# Optimizing a Trainium2 kernel written in Bass

```python
import numpy as np
import jax
import jax.numpy as jnp

def _softmax(x, axis=-1):
    return jax.nn.softmax(x, axis=axis)
def _gelu(x):
    return jax.nn.gelu(x, approximate=True)
def _silu(x):
    return jax.nn.silu(x)
def _sigmoid(x):
    return jax.nn.sigmoid(x)
def _layernorm(x, axis=-1, eps=1e-5):
    m = jnp.mean(x, axis=axis, keepdims=True)
    v = jnp.var(x, axis=axis, keepdims=True)
    return (x - m) / jnp.sqrt(v + eps)
def _scatter_add(tgt, idx, src, axis=0):
    return tgt.at[idx].add(src)
def _segment_sum(src, seg, n):
    return jax.ops.segment_sum(src, seg, n)

kernel_name = 'mk_adj_preln_d1_adj_256_0c8b20'

def setup_inputs(seed: int = 0):
    np.random.seed(seed)
    _w = jnp.asarray
    def _rec_inputs():
        import jax
        import jax.numpy as jnp
        _gk = jax.random.key(seed)
        x = -0.0002928 + 1 * jax.random.normal(jax.random.fold_in(_gk, 1), (8192, 256), jnp.float32)
        _a = jax.random.bernoulli(jax.random.fold_in(_gk, 2), 0.00195312, (8192, 8192))
        adj = _a.astype(jnp.int32)
        return x, adj
    x, adj = _rec_inputs()
    def _L0_gnn_setup():
        import jax, jax.numpy as jnp
        import numpy as np
        N = 16384
        F_IN = 256
        F_OUT = 256
        key = jax.random.key(seed)
        k1, k2, k3 = jax.random.split(key, 3)
        x = jax.random.normal(k1, (N, F_IN), dtype=jnp.float32)
        adj = jax.random.randint(k2, (N, N), 0, 2, dtype=jnp.int32)
        stdv = np.sqrt(6.0 / (2 * F_IN + F_OUT)).astype(np.float32)
        weight = jax.random.uniform(k3, (2 * F_IN, F_OUT), dtype=jnp.float32, minval=-stdv, maxval=stdv)
        bias = jnp.zeros((F_OUT,), dtype=jnp.float32)
        return {'x': x, 'adj': adj, 'weight': weight, 'bias': bias}
    _L0_gnn_all = _L0_gnn_setup()
    _L0_gnn_in = {k: v for k, v in _L0_gnn_all.items() if k in ('weight', 'bias', )}
    del _L0_gnn_all

    return {
        "x": x,
        "adj": adj,
        "L0_gnn_weight": _L0_gnn_in["weight"],
        "L0_gnn_bias": _L0_gnn_in["bias"],
    }

def reference(x, adj, L0_gnn_weight, L0_gnn_bias):
    import jax
    import jax.numpy as jnp
    def _L0_gnn_ref(x, adj, weight, bias):
        import jax, jax.numpy as jnp
        import numpy as np
        N = 16384
        F_IN = 256
        F_OUT = 256
        a = adj.astype(x.dtype)
        deg = jnp.sum(a, axis=1, keepdims=True)
        x1 = a @ x / deg
        n_x = jnp.concatenate([x1, x], axis=1)
        return n_x @ weight + bias

    h = jnp.maximum(_layernorm(x, axis=-1), 0.0)
    x = x + _L0_gnn_ref(h, adj, L0_gnn_weight, L0_gnn_bias)
    return x


_drawn_inputs = setup_inputs


def setup_inputs(seed=0):
    import zlib

    import numpy as np

    out = dict(_drawn_inputs(seed))
    spreads = {'L0_gnn_bias': (0.0, 0.1)}
    factors = {}
    for name, (base, spread) in spreads.items():
        noise = np.random.default_rng([zlib.crc32(name.encode()), seed]).standard_normal(out[name].shape)
        drawn = base * np.exp(spread * noise) if base else spread * noise
        out[name] = jnp.asarray(drawn.astype(out[name].dtype))
    for name, factor in factors.items():
        out[name] = (out[name] * factor).astype(out[name].dtype)
    return out
```

```python
import concourse.bass as bass
from concourse import mybir
from contextlib import ExitStack


def graph_layer_kernel(nc: bass.Bass, x: bass.AP, adj: bass.AP, weight: bass.AP, bias: bass.AP, out: bass.AP):
    fp32, fp16 = mybir.dt.float32, mybir.dt.float16
    i32, u32 = mybir.dt.int32, mybir.dt.uint32
    ALU = mybir.AluOpType
    ACT = mybir.ActivationFunctionType

    P = 128
    N, F = x.shape
    FO = weight.shape[1]
    Q = 4
    K = P // Q
    NT = N // P
    PAIRS = NT // 2
    C = N // Q
    FC = F // P
    SCALE = 2.0 ** 11
    EPS = 1e-5
    XB = 8
    NB = NT // XB
    NX = 3
    assert Q == 4 and F == 256 and FO == 256 and F * SCALE ** 2 < 65504 ** 2 and NB == 2 * Q

    adj_v = adj.rearrange("(g t k e) (q c) -> t e q k g c", g=Q, k=K, e=2, q=Q)
    x_v = x.rearrange("(g t k e) f -> t e g k f", g=Q, k=K, e=2)
    out_v = out.rearrange("(g t k e) f -> t e g k f", g=Q, k=K, e=2)
    xb_v = x.rearrange("(g b t k e) f -> b g k t (e f)", g=Q, b=NB, k=K, e=2)

    ctx = ExitStack()
    with ctx:
        def sb(name, shape, dt):
            return ctx.enter_context(nc.sbuf_tensor(name, shape, dt))

        def ps(name, shape, dt):
            return ctx.enter_context(nc.psum_tensor(name, shape, dt))

        def sem(name):
            return ctx.enter_context(nc.semaphore(name))

        hparts = sb("hparts", [P, NT, 2 * F], fp16)
        stage = sb("stage", [P, 2, 2, 2, C], i32)
        cast = sb("cast", [P, 2, C], fp16)
        adjT = sb("adjT", [P, 2, PAIRS, Q, K], u32)
        work = sb("work", [P, NX * XB * F + 768], fp32)
        xb = work[:, 0:NX * XB * F].rearrange("p (n t f) -> p n t f", n=NX, t=XB)
        o = (NX - 1) * XB * F
        xt = work[:, o:o + 2 * F].rearrange("p (n f) -> p n f", n=2)
        res = work[:, o + 2 * F:o + 4 * F].rearrange("p (n f) -> p n f", n=2)
        agg = work[:, o + 4 * F:o + 6 * F].rearrange("p (n f) -> p n f", n=2)
        tsb = work[:, o + 6 * F:o + 10 * F].rearrange("p (n c m) -> p n c m", n=2, c=2 * FC)
        low = work[:, o + 10 * F:o + 11 * F]
        wsb = sb("wsb", [P, 2 * FC, FO], fp32)
        biasb = sb("biasb", [P, FO], fp32)
        ident = sb("ident", [P, P], fp32)
        ident_s = sb("ident_s", [P, P], fp16)
        fold = sb("fold", [P, P], fp32)
        gmask = sb("gmask", [P, Q], fp32)
        rowsum = sb("rowsum", [P, 2, Q], fp32)
        degq = sb("degq", [P, Q], fp32)
        deg = sb("deg", [P, 1], fp32)
        rdeg = sb("rdeg", [P, 2], fp32)
        stats = sb("stats", [P, 2, XB, 6], fp32)
        mv = sb("mv", [P, 2, XB, 2], fp32)
        var = sb("var", [P, 2, XB], fp32)
        std = sb("std", [P, 2, XB], fp32)
        r0 = sb("r0", [P, 2, XB], fp32)
        r1 = sb("r1", [P, 2, XB], fp32)
        rs = sb("rs", [P, 2, XB], fp32)
        nb = sb("nb", [P, 2, XB], fp32)

        p_agg = [ps(f"p_agg{i}", [P, 2 * F], fp32) for i in range(2)]
        p_t = [ps(f"p_t{i}", [P, 2 * FC, P], fp32) for i in range(2)]
        p_out = [ps(f"p_out{i}", [P, 512], fp32) for i in range(2)]
        p_deg = ps("p_deg", [P, 512], fp32)

        adj16 = adjT[:, :, :, :, :].bitcast(fp16).rearrange("p s t g (k e) -> p s t (g k) e", e=2)
        cast32 = cast[:, :, :].bitcast(u32)

        x_in = [sem(f"x_in{i}") for i in range(NX)]
        w_in = sem("w_in")
        staged = [[sem(f"staged{e}{h}") for h in range(2)] for e in range(2)]
        consts = sem("consts")
        cstep = sem("cstep")
        stats_v = sem("stats_v")
        std_ready = sem("std_ready")
        norm_ready = sem("norm_ready")
        relu_done = sem("relu_done")
        high_done = sem("high_done")
        h_ready = sem("h_ready")
        cast_done = sem("cast_done")
        group_done = sem("group_done")
        deg_done = sem("deg_done")
        deg_read = sem("deg_read")
        deg_sum = sem("deg_sum")
        rdeg_ready = sem("rdeg_ready")
        agg_done = sem("agg_done")
        low_ready = sem("low_ready")
        agg_ready = sem("agg_ready")
        t_done = sem("t_done")
        t_ready = sem("t_ready")
        out_done = sem("out_done")
        fin_done = sem("fin_done")
        xt_in = [sem(f"xt_in{e}") for e in range(2)]
        xt_ready = sem("xt_ready")
        sent = [sem(f"sent{e}") for e in range(2)]
        vstep = sem("vstep")

        def after(eng, s, v):
            if not isinstance(v, int) or v > 0:
                eng.wait_ge(s, v)

        block = ctx.enter_context(nc.Block())

        @block.sync
        def _(sp):
            def load_x(b):
                if b >= NX:
                    sp.wait_ge(h_ready, b - NX + 1)
                for g in (0, 2, 1, 3):
                    sp.dma_start(xb[K * g:K * g + K, b % NX].rearrange("p (t e) f -> p t (e f)", e=2),
                                 xb_v[b, g]).then_inc(x_in[b % NX], 16)

            def load_adj(t, e, h):
                for q in (0, 2, 1, 3):
                    sp.dma_start(stage[K * q:K * q + K, e, h, :, :],
                                 adj_v[t, e, q, :, 2 * h:2 * h + 2, :]).then_inc(staged[e][h], 16)

            def load_adj_pair(t):
                for e in range(2):
                    for h in range(2):
                        after(sp, cast_done, t * 8 + (4 * e + 2 * h + 2 - 8))
                        load_adj(t, e, h)

            def load_xt_pair(t):
                for e in range(2):
                    after(sp, fin_done, t * 2 + (e - 1))
                    for g in range(Q):
                        sp.dma_start(xt[K * g:K * g + K, e, :], x_v[t, e, g]).then_inc(xt_in[e], 16)

            load_x(0)
            load_x(1)
            sp.dma_start(wsb[:, :, :], weight.rearrange("(c p) f -> p c f", p=P)).then_inc(w_in, 16)
            sp.dma_start(biasb[:, :], bias.rearrange("(a f) -> a f", a=1).broadcast_to([P, FO])).then_inc(w_in, 16)
            load_adj(0, 0, 0)
            load_x(2)
            load_adj(0, 0, 1)
            load_x(3)
            load_adj(0, 1, 0)
            load_x(4)
            load_adj(0, 1, 1)
            for b in range(5, NB):
                load_x(b)
            load_adj_pair(1)
            sp.wait_ge(h_ready, NB)
            load_xt_pair(0)
            with sp.Fori(2, PAIRS) as t:
                load_adj_pair(t)
                load_xt_pair(t - 1)
            load_xt_pair(PAIRS - 1)

        @block.gpsimd
        def _(pool):
            made = [0]

            def step(ins):
                made[0] += 1
                ins.then_inc(cstep, 1)
                pool.wait_ge(cstep, made[0])

            step(pool.memset(ident[:, :], 0.0))
            step(pool.memset(ident_s[:, :], 0.0))
            step(pool.memset(fold[:, :], 0.0))
            step(pool.memset(gmask[:, :], 0.0))
            for m, fill, d in [(ident, 1.0, 0), (ident_s, 1.0 / SCALE, 0)] + \
                    [(fold, 1.0, d) for d in range(1 - Q, Q)]:
                step(pool.affine_select(out=m[:, :], in_=m[:, :], compare_op=ALU.not_equal, fill=fill,
                                        base=-K * d, pattern=[[-1, P]], channel_multiplier=1))
            for g in range(Q):
                last = pool.memset(gmask[K * g:K * g + K, g:g + 1], SCALE)
            last.then_inc(consts, 1)

            for b in range(NB):
                pool.wait_ge(high_done, b + 1)
                hp = hparts[:, XB * b:XB * b + XB, :]
                pool.tensor_tensor(hp[:, :, F:2 * F], xb[:, b % NX], hp[:, :, 0:F],
                                   ALU.subtract).then_inc(h_ready, 1)

            pool.wait_ge(w_in, 32)

            def add_bias(t, e):
                pool.wait_ge(xt_in[e], t * (16 * Q) + 16 * Q)
                pool.tensor_tensor(xt[:, e, :], xt[:, e, :], biasb[:, :], ALU.add).then_inc(xt_ready, 1)

            def send(t, e):
                pool.wait_ge(fin_done, t * 2 + (e + 1))
                for g in range(Q):
                    pool.dma_start(out_v[t, e, g], res[K * g:K * g + K, e, :]).then_inc(sent[e], 16)

            add_bias(0, 0)
            add_bias(0, 1)
            with pool.Fori(1, PAIRS) as t:
                for e in range(2):
                    send(t - 1, e)
                    add_bias(t, e)
            for e in range(2):
                send(PAIRS - 1, e)
            for e in range(2):
                pool.wait_ge(sent[e], 16 * Q * PAIRS)

        @block.scalar
        def _(act):
            def sqrt_var(b):
                act.wait_ge(stats_v, b + 1)
                nc.scalar.activation(std[:, b % 2], var[:, b % 2], ACT.Sqrt).then_inc(std_ready, 1)

            def relu(b):
                act.wait_ge(norm_ready, b + 1)
                for i in range(XB):
                    last = nc.scalar.activation(xb[:, b % NX, i], xb[:, b % NX, i], ACT.Relu,
                                                bias=nb[:, b % 2, i:i + 1], scale=rs[:, b % 2, i:i + 1])
                last.then_inc(relu_done, 1)

            def cast_group(t, e, g):
                if g % 2 == 0:
                    act.wait_ge(staged[e][g // 2], t * (16 * Q) + 16 * Q)
                after(act, group_done, t * 8 + (4 * e + g - 1))
                if g == 0:
                    after(act, deg_done, t * 2 + (e - 1))
                nc.scalar.activation(cast[:, g % 2], stage[:, e, g // 2, g % 2], ACT.Copy,
                                     accum_out=rowsum[:, e, g:g + 1]).then_inc(cast_done, 1)

            def scale_low(t, e):
                act.wait_ge(agg_done, t * 2 + (e + 1))
                act.wait_ge(rdeg_ready, t * 2 + (e + 1))
                after(act, agg_ready, t * 2 + e)
                nc.scalar.activation(low, p_agg[e][:, F:2 * F], ACT.Copy,
                                     scale=rdeg[:, e:e + 1]).then_inc(low_ready, 1)

            def copy_t(t, e):
                act.wait_ge(t_done, t * 2 + (e + 1))
                after(act, out_done, t * 2 + (e - 1))
                nc.scalar.activation(tsb[:, e], p_t[e][:, :, :], ACT.Copy).then_inc(t_ready, 1)

            def tile(t, e):
                cast_group(t, e, 0)
                cast_group(t, e, 1)
                scale_low(t - 1, e)
                cast_group(t, e, 2)
                cast_group(t, e, 3)
                copy_t(t - 1, e)

            sqrt_var(0)
            for b in range(NB):
                relu(b)
                if b + 1 < NB:
                    sqrt_var(b + 1)
                cast_group(0, b // Q, b % Q)
            tile(1, 0)
            tile(1, 1)
            with act.Fori(2, PAIRS) as t:
                tile(t, 0)
                tile(t, 1)
            for e in range(2):
                scale_low(PAIRS - 1, e)
                copy_t(PAIRS - 1, e)

        @block.vector
        def _(dve):
            steps = [0]

            def step(ins):
                steps[0] += 1
                ins.then_inc(vstep, 1)
                dve.wait_ge(vstep, steps[0])

            def norm_stats(b):
                dve.wait_ge(x_in[b % NX], (b // NX + 1) * 16 * Q)
                s = b % 2
                for i in range(XB):
                    last = nc.vector.bn_stats(stats[:, s, i], xb[:, b % NX, i])
                step(last)
                for i in range(XB):
                    last = nc.vector.bn_aggr(mv[:, s, i], stats[:, s, i])
                step(last)
                nc.vector.tensor_scalar(var[:, s], mv[:, s, :, 1], EPS, None, ALU.add).then_inc(stats_v, 1)

            def norm_scale(b):
                s = b % 2
                dve.wait_ge(std_ready, b + 1)
                if b >= 2:
                    dve.wait_ge(relu_done, b - 1)
                step(nc.vector.reciprocal(r0[:, s], std[:, s]))
                step(nc.vector.tensor_tensor(r1[:, s], r0[:, s], r0[:, s], ALU.mult))
                step(nc.vector.tensor_tensor(r1[:, s], r1[:, s], var[:, s], ALU.mult))
                step(nc.vector.tensor_scalar(r1[:, s], r1[:, s], -0.5 * SCALE, 1.5 * SCALE, ALU.mult, ALU.add))
                step(nc.vector.tensor_tensor(rs[:, s], r1[:, s], r0[:, s], ALU.mult))
                nc.vector.scalar_tensor_tensor(out=nb[:, s], in0=mv[:, s, :, 0], scalar=-1.0, in1=rs[:, s],
                                               op0=ALU.mult, op1=ALU.mult).then_inc(norm_ready, 1)

            def high_part(b):
                dve.wait_ge(relu_done, b + 1)
                nc.vector.tensor_copy(hparts[:, XB * b:XB * b + XB, 0:F], xb[:, b % NX]).then_inc(high_done, 1)

            def transpose_group(t, e, g):
                dve.wait_ge(cast_done, t * 8 + (4 * e + g + 1))
                if g == 0:
                    after(dve, agg_done, t * 2 + (e - 1))
                nc.vector.transpose(adjT[:, e, :, g, :], cast32[:, g % 2].rearrange("p (t k) -> p t k", k=K))\
                  .then_inc(group_done, 1)

            def degree(t, e):
                dve.wait_ge(deg_done, t * 2 + (e + 1))
                nc.vector.tensor_tensor(degq[:, :], p_deg[:, 0:Q], gmask[:, :], ALU.mult).then_inc(deg_read, 1)
                dve.wait_ge(deg_read, t * 2 + (e + 1))
                nc.vector.reduce_sum(deg[:, :], degq[:, :], axis=mybir.AxisListType.X).then_inc(deg_sum, 1)
                dve.wait_ge(deg_sum, t * 2 + (e + 1))
                nc.vector.reciprocal(rdeg[:, e:e + 1], deg[:, :]).then_inc(rdeg_ready, 1)

            def scale_high(t, e):
                dve.wait_ge(low_ready, t * 2 + (e + 1))
                after(dve, t_done, t * 2 + (e - 1))
                nc.vector.scalar_tensor_tensor(out=agg[:, e], in0=p_agg[e][:, 0:F], scalar=rdeg[:, e:e + 1],
                                               in1=low, op0=ALU.mult, op1=ALU.add).then_inc(agg_ready, 1)

            def finish(t, e):
                dve.wait_ge(out_done, t * 2 + (e + 1))
                dve.wait_ge(xt_ready, t * 2 + (e + 1))
                after(dve, sent[e], t * (16 * Q))
                nc.vector.tensor_tensor(res[:, e], p_out[e][:, 0:FO], xt[:, e], ALU.add).then_inc(fin_done, 1)

            def tile(t, e, finishing=True):
                transpose_group(t, e, 0)
                scale_high(t - 1, e)
                transpose_group(t, e, 1)
                degree(t - 1 + e, 1 - e)
                transpose_group(t, e, 2)
                transpose_group(t, e, 3)
                if finishing:
                    finish(t - 2 + e, 1 - e)

            dve.wait_ge(consts, 1)
            norm_stats(0)
            norm_scale(0)
            for b in range(NB):
                if b + 1 < NB:
                    norm_stats(b + 1)
                    norm_scale(b + 1)
                high_part(b)
                transpose_group(0, b // Q, b % Q)
            degree(0, 0)
            tile(1, 0, finishing=False)
            tile(1, 1)
            tile(2, 0)
            tile(2, 1)
            with dve.Fori(3, PAIRS) as t:
                tile(t, 0)
                tile(t, 1)
            T = PAIRS
            scale_high(T - 1, 0)
            degree(T - 1, 1)
            finish(T - 2, 1)
            scale_high(T - 1, 1)
            finish(T - 1, 0)
            finish(T - 1, 1)

        @block.tensor
        def _(pe):
            def products(e, tiles):
                for j in tiles:
                    last = nc.tensor.matmul(p_agg[e][:, :], adj16[:, e, j // 2, :, j % 2], hparts[:, j, :],
                                            start=(j == 0), stop=(j == NT - 1))
                if tiles[-1] == NT - 1:
                    last.then_inc(agg_done, 1)

            def degree(t, e):
                pe.wait_ge(cast_done, t * 8 + (4 * e + 4))
                after(pe, deg_read, t * 2 + e)
                nc.tensor.matmul(p_deg[:, 0:Q], fold[:, :], rowsum[:, e, :], start=True, stop=True)\
                  .then_inc(deg_done, 1)

            def transpose_h(t, e):
                after(pe, t_ready, t * 2 + (e - 1))
                for c in range(FC):
                    for part in range(2):
                        nc.tensor.matmul(p_t[e][:, FC + c, :],
                                         hparts[:, t * 2 + e, part * F + c * P:part * F + (c + 1) * P],
                                         ident_s[:, :], start=(part == 0), stop=(part == 1))

            def transpose_agg(t, e):
                pe.wait_ge(agg_ready, t * 2 + (e + 1))
                for c in range(FC):
                    last = nc.tensor.transpose(p_t[e][:, c, :], agg[:, e, c * P:(c + 1) * P], ident[:, :])
                last.then_inc(t_done, 1)

            def weigh(t, e):
                pe.wait_ge(t_ready, t * 2 + (e + 1))
                after(pe, fin_done, t * 2 + (e - 1))
                for c in range(2 * FC):
                    last = nc.tensor.matmul(p_out[e][:, 0:FO], tsb[:, e, c, :], wsb[:, c, :],
                                            start=(c == 0), stop=(c == 2 * FC - 1))
                last.then_inc(out_done, 1)

            def tile(t, e, work):
                pe.wait_ge(group_done, t * 8 + (4 * e + 4))
                degree(t, e)
                at = 0
                for j, job in work:
                    products(e, range(at, j))
                    job()
                    at = j
                products(e, range(at, NT))

            def steady(t, e):
                tile(t, e, [(20, lambda: transpose_agg(t - 1 + e, 1 - e)),
                            (44, lambda: weigh(t - 1 + e, 1 - e)),
                            (50, lambda: transpose_h(t, e))])

            pe.wait_ge(consts, 1)
            pe.wait_ge(w_in, 32)
            pe.wait_ge(group_done, Q)
            degree(0, 0)
            for b in range(NB):
                pe.wait_ge(h_ready, b + 1)
                tiles = range(XB * b, XB * b + XB)
                if b < NB - 2:
                    products(0, tiles)
            pe.wait_ge(group_done, 2 * Q)
            for b in range(NB - 2, NB):
                products(0, range(XB * b, XB * b + XB))
            for b in range(NB):
                products(1, range(XB * b, XB * b + XB))
            degree(0, 1)
            transpose_h(0, 0)
            transpose_h(0, 1)
            tile(1, 0, [(16, lambda: transpose_agg(0, 0)), (40, lambda: weigh(0, 0)),
                        (44, lambda: transpose_agg(0, 1)), (60, lambda: transpose_h(1, 0))])
            tile(1, 1, [(4, lambda: weigh(0, 1)), (20, lambda: transpose_agg(1, 0)),
                        (44, lambda: weigh(1, 0)), (50, lambda: transpose_h(1, 1))])
            with pe.Fori(2, PAIRS) as t:
                steady(t, 0)
                steady(t, 1)
            transpose_agg(PAIRS - 1, 1)
            weigh(PAIRS - 1, 1)


_INS = ['x', 'adj', 'L0_gnn_weight', 'L0_gnn_bias']
_OUTS = [((8192, 256), 'float32')]


def kernel(**inputs):
    import numpy as _np
    import concourse.bacc as _bacc
    from concourse import mybir as _mybir
    from concourse.bass_utils import run_bass_kernel_spmd as _run

    nc = _bacc.Bacc("TRN2", target_bir_lowering=False, num_devices=1)
    arrays, args = {}, []
    for name in _INS:
        a = _np.ascontiguousarray(inputs[name])
        arrays[f"in_{name}_dram"] = a
        args.append(nc.dram_tensor(f"in_{name}_dram", a.shape, _mybir.dt.from_np(a.dtype), kind="ExternalInput").ap())
    for i, (shape, dtype) in enumerate(_OUTS):
        dt = _mybir.dt.from_np(_np.dtype(dtype))
        args.append(nc.dram_tensor(f"out_{i}_dram", shape, dt, kind="ExternalOutput").ap())
    graph_layer_kernel(nc, *args)
    r = _run(nc, [arrays], core_ids=[0])
    return r.results[0]["out_0_dram"]
```

```python
import concourse.bass as bass
from concourse import mybir
from contextlib import ExitStack


def graph_layer_kernel(nc: bass.Bass, x: bass.AP, adj: bass.AP, weight: bass.AP, bias: bass.AP, out: bass.AP):
    fp32, fp16, bf16 = mybir.dt.float32, mybir.dt.float16, mybir.dt.bfloat16
    i32, u32 = mybir.dt.int32, mybir.dt.uint32
    ALU = mybir.AluOpType
    ACT = mybir.ActivationFunctionType

    P = 128
    N, F = x.shape
    FO = weight.shape[1]
    Q = 4
    K = P // Q
    NT = N // P
    PAIRS = NT // 2
    C = N // Q
    FC = F // P
    SCALE = 2.0 ** 11
    EPS = 1e-5
    XB = 8
    NB = NT // XB
    NX = 3
    ORDER = [('x', 3), ('adj', 0), ('x', 4), ('adj', 1), ('x', 5), ('x', 6), ('adj', 2), ('x', 7), ('adj', 3)]
    WITH = [[], [0, 1], [], [2, 3], [], [4, 5], [6, 7], []]
    assert Q == 4 and F == 256 and FO == 256 and F * SCALE ** 2 < 65504 ** 2 and len(WITH) == NB

    adj_v = adj.rearrange("(g t k e) (q c) -> t e q k g c", g=Q, k=K, e=2, q=Q)
    xt_v = x.rearrange("(g t k e) f -> t g k e f", g=Q, k=K, e=2)
    out_v = out.rearrange("(g t k e) f -> t g k e f", g=Q, k=K, e=2)
    xb_v = x.rearrange("(g b t k e) f -> b g k t (e f)", g=Q, b=NB, k=K, e=2)

    ctx = ExitStack()
    with ctx:
        def sb(name, shape, dt):
            return ctx.enter_context(nc.sbuf_tensor(name, shape, dt))

        def ps(name, shape, dt):
            return ctx.enter_context(nc.psum_tensor(name, shape, dt))

        def sem(name):
            return ctx.enter_context(nc.semaphore(name))

        hparts = sb("hparts", [P, NT, 2 * F], fp16)
        stage = sb("stage", [P, 2, 2, 2, C], i32)
        cast = sb("cast", [P, 2, C], fp16)
        adjT = sb("adjT", [P, 2, PAIRS, Q, K], u32)
        work = sb("work", [P, NX * XB * F], fp32)
        xwork = work[:, :].rearrange("p (n t f) -> p n t f", n=NX, t=XB)
        xadj = adjT[:, 1].rearrange("p t g k -> p (t g k)").bitcast(fp32).rearrange("p (n t f) -> p n t f", n=2, t=XB)
        xb = [xwork[:, b] for b in range(NX)] + [xadj[:, 0], xadj[:, 1]] + [xwork[:, b] for b in range(NX)]
        xt = work[:, 0:2 * F].rearrange("p (n f) -> p n f", n=2)
        res = work[:, 2 * F:4 * F].rearrange("p (n f) -> p n f", n=2)
        aggp = work[:, 4 * F:6 * F].bitcast(fp16).rearrange("p (n a f) -> p n a f", n=2, a=2)
        tsb = work[:, 6 * F:10 * F].bitcast(fp16).rearrange("p (n c a m) -> p n c a m", n=2, c=2 * FC, a=2)
        low = work[:, 10 * F:11 * F]
        aggf = work[:, 11 * F:12 * F]
        wsb = sb("wsb", [P, 2 * FC, FO], fp32)
        biasb = sb("biasb", [P, 2, FO], fp32)
        wparts = sb("wparts", [P, 2 * FC, 2, FO], fp16)
        wmax = sb("wmax", [P, 1], fp32)
        wtop = sb("wtop", [P, 1], fp32)
        wpow = sb("wpow", [P, 1], fp32)
        wrec = sb("wrec", [P, 1], fp32)
        wscale = sb("wscale", [P, 1], fp32)
        unscale = sb("unscale", [P, 1], fp32)
        ident = sb("ident", [P, P], fp16)
        fold = sb("fold", [P, P], bf16)
        gmask = sb("gmask", [P, 3, Q], fp32)
        rowsum = sb("rowsum", [P, 2, Q], fp32)
        rest = sb("rest", [P, 2, Q], fp32)
        sumparts = sb("sumparts", [P, 2, 3, Q], bf16)
        zero = sb("zero", [P, Q], fp32)
        degq = sb("degq", [P, 3 * Q], fp32)
        deg = sb("deg", [P, 1], fp32)
        rdeg = sb("rdeg", [P, 2], fp32)
        stats = sb("stats", [P, 2, XB, 6], fp32)
        mv = sb("mv", [P, NB, XB, 2], fp32)
        var = sb("var", [P, NB, XB], fp32)
        mneg = sb("mneg", [P, NB, XB], fp32)
        std = sb("std", [P, NB, XB], fp32)
        r0 = sb("r0", [P, NB, XB], fp32)
        r1 = sb("r1", [P, NB, XB], fp32)
        rs = sb("rs", [P, NB, XB], fp32)
        nb = sb("nb", [P, NB, XB], fp32)

        p_agg = [ps(f"p_agg{i}", [P, 2 * F], fp32) for i in range(2)]
        p_t = [ps(f"p_t{i}", [P, 2 * FC, 2, P], fp16) for i in range(2)]
        p_out = [ps(f"p_out{i}", [P, 512], fp32) for i in range(2)]
        p_deg = ps("p_deg", [P, 512], fp32)

        adj16 = adjT[:, :, :, :, :].bitcast(fp16).rearrange("p s t g (k e) -> p s t (g k) e", e=2)
        cast32 = cast[:, :, :].bitcast(u32)

        x_in = [sem(f"x_in{b}") for b in range(NB)]
        w_in = sem("w_in")
        staged = [[sem(f"staged{e}{h}") for h in range(2)] for e in range(2)]
        consts = sem("consts")
        cstep = sem("cstep")
        stats_v = sem("stats_v")
        std_ready = sem("std_ready")
        recip_ready = sem("recip_ready")
        wmax_ready = sem("wmax_ready")
        wtop_ready = sem("wtop_ready")
        wscale_ready = sem("wscale_ready")
        w_ready = sem("w_ready")
        norm_ready = sem("norm_ready")
        relu_done = sem("relu_done")
        high_done = sem("high_done")
        h_ready = sem("h_ready")
        cast_done = sem("cast_done")
        group_done = sem("group_done")
        sums_split = sem("sums_split")
        deg_done = sem("deg_done")
        deg_read = sem("deg_read")
        deg_sum = sem("deg_sum")
        rdeg_ready = sem("rdeg_ready")
        agg_done = sem("agg_done")
        low_ready = sem("low_ready")
        agg_sum = sem("agg_sum")
        agg_high = sem("agg_high")
        agg_ready = sem("agg_ready")
        t_done = sem("t_done")
        t_ready = sem("t_ready")
        out_done = sem("out_done")
        fin_done = sem("fin_done")
        xt_in = sem("xt_in")
        xt_ready = sem("xt_ready")
        sent = sem("sent")
        last_sent = sem("last_sent")
        split_step = sem("split_step")
        vstep = sem("vstep")

        def after(eng, s, v):
            if not isinstance(v, int) or v > 0:
                eng.wait_ge(s, v)

        def load_adj(eng, t, e, h, quadrants):
            for q in quadrants:
                eng.dma_start(stage[K * q:K * q + K, e, h, :, :],
                              adj_v[t, e, q, :, 2 * h:2 * h + 2, :]).then_inc(staged[e][h], 16)

        block = ctx.enter_context(nc.Block())

        @block.sync
        def _(sp):
            def load_x(b):
                if b >= NX + 2:
                    sp.wait_ge(h_ready, b - NX - 1)
                for g in (0, 2, 1, 3):
                    sp.dma_start(xb[b][K * g:K * g + K].rearrange("p (t e) f -> p t (e f)", e=2),
                                 xb_v[b, g]).then_inc(x_in[b], 16)

            def load_tile(t, e, quadrants=(0, 1)):
                for h in range(2):
                    sp.wait_ge(cast_done, t * 8 + (4 * e + 2 * h + 2 - 8))
                    load_adj(sp, t, e, h, quadrants)

            def load_xt(t):
                after(sp, fin_done, t * 2)
                for g in range(Q):
                    sp.dma_start(xt[K * g:K * g + K], xt_v[t, g]).then_inc(xt_in, 16)

            load_x(0)
            load_x(1)
            load_x(2)
            for kind, i in ORDER:
                if kind == "x":
                    load_x(i)
                else:
                    load_adj(sp, 0, i // 2, i % 2, (0, 2, 1, 3))
            sp.dma_start(wsb[:, :, :], weight.rearrange("(c p) f -> p c f", p=P)).then_inc(w_in, 16)
            for e in range(2):
                sp.dma_start(biasb[:, e], bias.rearrange("(a f) -> a f", a=1).broadcast_to([P, FO])).then_inc(w_in, 16)
            load_tile(1, 0, (0, 2, 1, 3))
            load_tile(1, 1, (0, 2, 1, 3))
            sp.wait_ge(h_ready, NB)
            load_xt(0)
            load_tile(2, 0)
            load_tile(2, 1)
            with sp.Fori(3, PAIRS) as t:
                load_tile(t, 0)
                load_xt(t - 2)
                load_tile(t, 1)
            load_xt(PAIRS - 2)
            load_xt(PAIRS - 1)
            for e in range(2):
                sp.wait_ge(fin_done, NT - 1 + e)
                for g in range(Q):
                    sp.dma_start(out_v[PAIRS - 1, g, :, e, :], res[K * g:K * g + K, e, :]).then_inc(last_sent, 16)
            sp.wait_ge(last_sent, 2 * 16 * Q)

        @block.gpsimd
        def _(pool):
            made = [0]

            def step(ins):
                made[0] += 1
                ins.then_inc(cstep, 1)
                pool.wait_ge(cstep, made[0])

            step(pool.memset(ident[:, :], 0.0))
            step(pool.memset(fold[:, :], 0.0))
            step(pool.memset(gmask[:, :, :], 0.0))
            step(pool.memset(zero[:, :], 0.0))
            for m, d in [(ident, 0)] + [(fold, d) for d in range(1 - Q, Q)]:
                step(pool.affine_select(out=m[:, :], in_=m[:, :], compare_op=ALU.not_equal, fill=1.0,
                                        base=-K * d, pattern=[[-1, P]], channel_multiplier=1))
            for g in range(Q):
                last = pool.memset(gmask[K * g:K * g + K, :, g], 1.0)
            last.then_inc(consts, 1)

            def norm_scale(b):
                pool.wait_ge(recip_ready, b + 1)
                step(pool.tensor_tensor(r1[:, b], r0[:, b], r0[:, b], ALU.mult))
                step(pool.tensor_tensor(r1[:, b], r1[:, b], var[:, b], ALU.mult))
                step(pool.tensor_scalar(r1[:, b], r1[:, b], -0.5 * SCALE, 1.5 * SCALE, ALU.mult, ALU.add))
                step(pool.tensor_tensor(rs[:, b], r1[:, b], r0[:, b], ALU.mult))
                pool.tensor_tensor(nb[:, b], mneg[:, b], rs[:, b], ALU.mult).then_inc(norm_ready, 1)

            def low_part(b):
                pool.wait_ge(high_done, b + 1)
                hp = hparts[:, XB * b:XB * b + XB, :]
                pool.tensor_tensor(hp[:, :, F:2 * F], xb[b], hp[:, :, 0:F],
                                   ALU.subtract).then_inc(h_ready, 1)

            def split_sums(t, e):
                pool.wait_ge(cast_done, t * 8 + (4 * e + 4))
                after(pool, deg_done, t * 2 + (e - 1))
                n = t * 8 + 4 * e
                rows, left, parts = rowsum[:, e], rest[:, e], sumparts[:, e]
                pool.tensor_tensor(parts[:, 0], rows, zero[:, :], ALU.add).then_inc(split_step, 1)
                pool.wait_ge(split_step, n + 1)
                pool.tensor_tensor(left, rows, parts[:, 0], ALU.subtract).then_inc(split_step, 1)
                pool.wait_ge(split_step, n + 2)
                pool.tensor_tensor(parts[:, 1], left, zero[:, :], ALU.add).then_inc(split_step, 1)
                pool.wait_ge(split_step, n + 3)
                pool.tensor_tensor(left, left, parts[:, 1], ALU.subtract).then_inc(split_step, 1)
                pool.wait_ge(split_step, n + 4)
                pool.tensor_tensor(parts[:, 2], left, zero[:, :], ALU.add).then_inc(sums_split, 1)

            norm_scale(0)
            for b in range(NB):
                if b + 1 < NB:
                    norm_scale(b + 1)
                low_part(b)
                if b == 3:
                    split_sums(0, 0)
                if b == NB - 2:
                    split_sums(0, 1)

            pool.wait_ge(wmax_ready, 1)
            pool.partition_all_reduce(wtop[:, :], wmax[:, :], P, bass.bass_isa.ReduceOp.max).then_inc(wtop_ready, 1)
            split_sums(1, 0)
            pool.wait_ge(wscale_ready, 1)
            step(pool.tensor_scalar(wsb[:, :, :], wsb[:, :, :], wscale[:, 0:1], None, ALU.mult))
            step(pool.tensor_copy(wparts[:, :, 0, :], wsb[:, :, :]))
            pool.tensor_tensor(wparts[:, :, 1, :], wsb[:, :, :], wparts[:, :, 0, :],
                               ALU.subtract).then_inc(w_ready, 1)

            def add_bias(t):
                pool.wait_ge(xt_in, t * (16 * Q) + 16 * Q)
                pool.tensor_tensor(xt[:, :, :], xt[:, :, :], biasb[:, :, :], ALU.add).then_inc(xt_ready, 1)

            def send(t):
                pool.wait_ge(fin_done, t * 2 + 2)
                for g in range(Q):
                    pool.dma_start(out_v[t, g], res[K * g:K * g + K]).then_inc(sent, 16)

            add_bias(0)
            split_sums(1, 1)
            with pool.Fori(2, PAIRS) as t:
                split_sums(t, 0)
                send(t - 2)
                add_bias(t - 1)
                split_sums(t, 1)
            send(PAIRS - 2)
            add_bias(PAIRS - 1)
            pool.wait_ge(sent, 16 * Q * (PAIRS - 1))

        @block.scalar
        def _(act):
            def sqrt_var(b):
                act.wait_ge(stats_v, b + 1)
                nc.scalar.activation(std[:, b], var[:, b], ACT.Sqrt).then_inc(std_ready, 1)

            def relu(b, part=range(XB)):
                act.wait_ge(norm_ready, b + 1)
                for i in part:
                    last = nc.scalar.activation(xb[b][:, i], xb[b][:, i], ACT.Relu,
                                                bias=nb[:, b, i:i + 1], scale=rs[:, b, i:i + 1])
                if part[-1] == XB - 1:
                    last.then_inc(relu_done, 1)

            def cast_group(t, e, g):
                if g % 2 == 0:
                    act.wait_ge(staged[e][g // 2], t * (16 * Q) + 16 * Q)
                after(act, group_done, t * 8 + (4 * e + g - 1))
                if g == 0:
                    after(act, sums_split, t * 2 + (e - 1))
                nc.scalar.activation(cast[:, g % 2], stage[:, e, g // 2, g % 2], ACT.Copy,
                                     accum_out=rowsum[:, e, g:g + 1]).then_inc(cast_done, 1)

            def scale_low(t, e):
                act.wait_ge(agg_done, t * 2 + (e + 1))
                act.wait_ge(rdeg_ready, t * 2 + (e + 1))
                after(act, agg_ready, t * 2 + e)
                nc.scalar.activation(low, p_agg[e][:, F:2 * F], ACT.Copy,
                                     scale=rdeg[:, e:e + 1]).then_inc(low_ready, 1)

            def copy_t(t, e):
                act.wait_ge(t_done, t * 2 + (e + 1))
                after(act, out_done, t * 2 + (e - 1))
                nc.scalar.activation(tsb[:, e], p_t[e][:, :, :, :], ACT.Copy).then_inc(t_ready, 1)

            def load_half(t, e, h):
                act.wait_ge(cast_done, t * 8 + (4 * e + 2 * h + 2 - 8))
                load_adj(act, t, e, h, (2, 3))

            def tile(t, e, loading=True):
                cast_group(t, e, 0)
                cast_group(t, e, 1)
                scale_low(t - 1, e)
                if loading:
                    load_half(t + 1, e, 0)
                cast_group(t, e, 2)
                cast_group(t, e, 3)
                copy_t(t - 1, e)
                if loading:
                    load_half(t + 1, e, 1)

            sqrt_var(0)
            relu(0, range(XB // 2))
            sqrt_var(1)
            relu(0, range(XB // 2, XB))
            for b in range(1, NB):
                if b + 1 < NB:
                    sqrt_var(b + 1)
                relu(b)
                for i in WITH[b]:
                    cast_group(0, i // Q, i % Q)
            tile(1, 0)
            tile(1, 1)
            with act.Fori(2, PAIRS - 1) as t:
                tile(t, 0)
                tile(t, 1)
            tile(PAIRS - 1, 0, loading=False)
            tile(PAIRS - 1, 1, loading=False)
            for e in range(2):
                scale_low(PAIRS - 1, e)
                copy_t(PAIRS - 1, e)

        @block.vector
        def _(dve):
            steps = [0]

            def step(ins):
                steps[0] += 1
                ins.then_inc(vstep, 1)
                dve.wait_ge(vstep, steps[0])

            def norm_stats(b):
                dve.wait_ge(x_in[b], 16 * Q)
                for i in range(XB):
                    last = nc.vector.bn_stats(stats[:, b % 2, i], xb[b][:, i])
                step(last)
                for i in range(XB):
                    last = nc.vector.bn_aggr(mv[:, b, i], stats[:, b % 2, i])
                step(last)
                nc.vector.tensor_scalar(var[:, b], mv[:, b, :, 1], EPS, None, ALU.add).then_inc(stats_v, 1)
                step(nc.vector.tensor_scalar(mneg[:, b], mv[:, b, :, 0], -1.0, None, ALU.mult))

            def recip_std(b):
                dve.wait_ge(std_ready, b + 1)
                nc.vector.reciprocal(r0[:, b], std[:, b]).then_inc(recip_ready, 1)

            def high_part(b):
                dve.wait_ge(relu_done, b + 1)
                nc.vector.tensor_copy(hparts[:, XB * b:XB * b + XB, 0:F], xb[b]).then_inc(high_done, 1)

            def transpose_group(t, e, g):
                dve.wait_ge(cast_done, t * 8 + (4 * e + g + 1))
                if g == 0:
                    after(dve, agg_done, t * 2 + (e - 1))
                nc.vector.transpose(adjT[:, e, :, g, :], cast32[:, g % 2].rearrange("p (t k) -> p t k", k=K))\
                  .then_inc(group_done, 1)

            def degree(t, e):
                dve.wait_ge(deg_done, t * 2 + (e + 1))
                nc.vector.tensor_tensor(degq[:, :], p_deg[:, 0:3 * Q], gmask[:, :, :].rearrange("p a g -> p (a g)"),
                                        ALU.mult).then_inc(deg_read, 1)
                dve.wait_ge(deg_read, t * 2 + (e + 1))
                nc.vector.reduce_sum(deg[:, :], degq[:, :], axis=mybir.AxisListType.X).then_inc(deg_sum, 1)
                dve.wait_ge(deg_sum, t * 2 + (e + 1))
                nc.vector.reciprocal(rdeg[:, e:e + 1], deg[:, :]).then_inc(rdeg_ready, 1)

            def scale_high(t, e):
                n = t * 2 + (e + 1)
                dve.wait_ge(low_ready, n)
                nc.vector.scalar_tensor_tensor(out=aggf, in0=p_agg[e][:, 0:F], scalar=rdeg[:, e:e + 1],
                                               in1=low, op0=ALU.mult, op1=ALU.add).then_inc(agg_sum, 1)
                dve.wait_ge(agg_sum, n)
                after(dve, t_done, t * 2 + (e - 1))
                nc.vector.tensor_copy(aggp[:, e, 0], aggf).then_inc(agg_high, 1)
                dve.wait_ge(agg_high, n)
                nc.vector.tensor_tensor(aggp[:, e, 1], aggf, aggp[:, e, 0], ALU.subtract).then_inc(agg_ready, 1)

            def scale_weight():
                dve.wait_ge(w_in, 48)
                nc.vector.tensor_reduce(wmax[:, :], wsb[:, :, :], mybir.AxisListType.XY, ALU.max,
                                        apply_absolute_value=True).then_inc(wmax_ready, 1)

            def scale_weight_factors():
                dve.wait_ge(wtop_ready, 1)
                step(nc.vector.tensor_scalar(wtop[:, :], wtop[:, :], 2.0 ** -100, None, ALU.max))
                step(nc.vector.tensor_scalar(wpow[:, :].bitcast(i32), wtop[:, :].bitcast(i32), 0x7F800000, None,
                                             ALU.bitwise_and))
                step(nc.vector.reciprocal(wrec[:, :], wpow[:, :]))
                step(nc.vector.tensor_scalar(unscale[:, :], wpow[:, :], 2.0 ** -14 / SCALE, None, ALU.mult))
                nc.vector.tensor_scalar(wscale[:, :], wrec[:, :], 2.0 ** 14, None, ALU.mult).then_inc(wscale_ready, 1)

            def finish(t, e):
                dve.wait_ge(out_done, t * 2 + (e + 1))
                if e == 0:
                    dve.wait_ge(xt_ready, t + 1)
                    after(dve, sent, t * (16 * Q))
                nc.vector.scalar_tensor_tensor(out=res[:, e], in0=p_out[e][:, 0:FO], scalar=unscale[:, 0:1],
                                               in1=xt[:, e], op0=ALU.mult, op1=ALU.add).then_inc(fin_done, 1)

            def tile(t, e, finishing=True):
                transpose_group(t, e, 0)
                scale_high(t - 1, e)
                transpose_group(t, e, 1)
                degree(t - 1 + e, 1 - e)
                transpose_group(t, e, 2)
                transpose_group(t, e, 3)
                if finishing:
                    finish(t - 2 + e, 1 - e)

            dve.wait_ge(consts, 1)
            norm_stats(0)
            recip_std(0)
            norm_stats(1)
            for b in range(NB):
                if b + 1 < NB:
                    recip_std(b + 1)
                if b + 2 < NB:
                    norm_stats(b + 2)
                high_part(b)
                for i in WITH[b]:
                    if i == Q:
                        degree(0, 0)
                        dve.wait_ge(h_ready, NX + 2)
                    transpose_group(0, i // Q, i % Q)
            scale_weight()
            tile(1, 0, finishing=False)
            scale_weight_factors()
            tile(1, 1)
            tile(2, 0)
            tile(2, 1)
            with dve.Fori(3, PAIRS) as t:
                tile(t, 0)
                tile(t, 1)
            T = PAIRS
            scale_high(T - 1, 0)
            degree(T - 1, 1)
            finish(T - 2, 1)
            scale_high(T - 1, 1)
            finish(T - 1, 0)
            finish(T - 1, 1)

        @block.tensor
        def _(pe):
            def products(e, tiles):
                for j in tiles:
                    last = nc.tensor.matmul(p_agg[e][:, :], adj16[:, e, j // 2, :, j % 2], hparts[:, j, :],
                                            start=(j == 0), stop=(j == NT - 1))
                if tiles[-1] == NT - 1:
                    last.then_inc(agg_done, 1)

            def degree(t, e):
                pe.wait_ge(sums_split, t * 2 + (e + 1))
                after(pe, deg_read, t * 2 + e)
                nc.tensor.matmul(p_deg[:, 0:3 * Q], fold[:, :], sumparts[:, e].rearrange("p a g -> p (a g)"),
                                 start=True, stop=True).then_inc(deg_done, 1)

            def transpose_h(t, e):
                after(pe, t_ready, t * 2 + (e - 1))
                for c in range(FC):
                    for part in range(2):
                        nc.tensor.transpose(p_t[e][:, FC + c, part, :],
                                            hparts[:, t * 2 + e, part * F + c * P:part * F + (c + 1) * P],
                                            ident[:, :])

            def transpose_agg(t, e):
                pe.wait_ge(agg_ready, t * 2 + (e + 1))
                for c in range(FC):
                    for part in range(2):
                        last = nc.tensor.transpose(p_t[e][:, c, part, :], aggp[:, e, part, c * P:(c + 1) * P],
                                                   ident[:, :])
                last.then_inc(t_done, 1)

            def weigh(t, e):
                pe.wait_ge(t_ready, t * 2 + (e + 1))
                after(pe, fin_done, t * 2 + (e - 1))
                terms = [(c, a, b) for c in range(2 * FC) for a, b in ((0, 0), (1, 0), (0, 1))]
                for n, (c, a, b) in enumerate(terms):
                    last = nc.tensor.matmul(p_out[e][:, 0:FO], tsb[:, e, c, a, :], wparts[:, c, b, :],
                                            start=(n == 0), stop=(n == len(terms) - 1))
                last.then_inc(out_done, 1)

            def first_weigh():
                pe.wait_ge(w_ready, 1)
                weigh(0, 0)

            def tile(t, e, work):
                pe.wait_ge(group_done, t * 8 + (4 * e + 4))
                at = 0
                for j, job in work:
                    products(e, range(at, j))
                    job()
                    at = j
                products(e, range(at, NT))

            def steady(t, e, last=False):
                tile(t, e, [(20, lambda: transpose_agg(t - 1 + e, 1 - e)),
                            (44, lambda: weigh(t - 1 + e, 1 - e)),
                            (50, lambda: transpose_h(t, e))] +
                     [(56, lambda: degree(t + e, 1 - e))] * (not last))

            pe.wait_ge(consts, 1)
            pe.wait_ge(group_done, Q)
            for b in range(NB - 2):
                pe.wait_ge(h_ready, b + 1)
                products(0, range(XB * b, XB * b + XB))
                if b == 1:
                    degree(0, 0)
            pe.wait_ge(group_done, 2 * Q)
            products(1, range(XB))
            degree(0, 1)
            for b in (NB - 2, NB - 1):
                pe.wait_ge(h_ready, b + 1)
                products(0, range(XB * b, XB * b + XB))
                if b == NB - 2:
                    products(1, range(XB, 3 * XB))
            products(1, range(3 * XB, NT))
            transpose_h(0, 0)
            transpose_h(0, 1)
            tile(1, 0, [(8, lambda: degree(1, 0)), (16, lambda: transpose_agg(0, 0)), (40, first_weigh),
                        (44, lambda: transpose_agg(0, 1)), (58, lambda: degree(1, 1)),
                        (60, lambda: transpose_h(1, 0))])
            tile(1, 1, [(4, lambda: weigh(0, 1)), (20, lambda: transpose_agg(1, 0)),
                        (44, lambda: weigh(1, 0)), (50, lambda: transpose_h(1, 1)),
                        (56, lambda: degree(2, 0))])
            with pe.Fori(2, PAIRS - 1) as t:
                steady(t, 0)
                steady(t, 1)
            steady(PAIRS - 1, 0)
            steady(PAIRS - 1, 1, last=True)
            transpose_agg(PAIRS - 1, 1)
            weigh(PAIRS - 1, 1)


_INS = ['x', 'adj', 'L0_gnn_weight', 'L0_gnn_bias']
_OUTS = [((8192, 256), 'float32')]


def kernel(**inputs):
    import numpy as _np
    import concourse.bacc as _bacc
    from concourse import mybir as _mybir
    from concourse.bass_utils import run_bass_kernel_spmd as _run

    nc = _bacc.Bacc("TRN2", target_bir_lowering=False, num_devices=1)
    arrays, args = {}, []
    for name in _INS:
        a = _np.ascontiguousarray(inputs[name])
        arrays[f"in_{name}_dram"] = a
        args.append(nc.dram_tensor(f"in_{name}_dram", a.shape, _mybir.dt.from_np(a.dtype), kind="ExternalInput").ap())
    for i, (shape, dtype) in enumerate(_OUTS):
        dt = _mybir.dt.from_np(_np.dtype(dtype))
        args.append(nc.dram_tensor(f"out_{i}_dram", shape, dt, kind="ExternalOutput").ap())
    graph_layer_kernel(nc, *args)
    r = _run(nc, [arrays], core_ids=[0])
    return r.results[0]["out_0_dram"]
```

```python
import concourse.bass as bass
from concourse import mybir
from contextlib import ExitStack


def graph_layer_kernel(nc: bass.Bass, x: bass.AP, adj: bass.AP, weight: bass.AP, bias: bass.AP, out: bass.AP):
    fp32, fp16, bf16 = mybir.dt.float32, mybir.dt.float16, mybir.dt.bfloat16
    i32, u32 = mybir.dt.int32, mybir.dt.uint32
    ALU = mybir.AluOpType
    ACT = mybir.ActivationFunctionType

    P = 128
    N, F = x.shape
    FO = weight.shape[1]
    Q = 4
    K = P // Q
    NT = N // P
    PAIRS = NT // 2
    C = N // Q
    FC = F // P
    SCALE = 2.0 ** 11
    EPS = 1e-5
    XB = 4
    NB = NT // XB
    STATS, NORM, RELU, HIGH, LOW, TRANS, EVAC, AGG = 7, 5, 4, 3, 3, 1, -1, -12
    STEPS = range(-STATS, PAIRS - EVAC)
    CAST_AT = {0: 0, 3: 1, 6: 2, 9: 3, 22: 4, 25: 5, 29: 6, 31: 7}
    DEG_AT = 12
    ORDER = [('x', b) for b in range(1, 6)] + [('adj', 0), ('x', 6), ('x', 7), ('adj', 1)] + \
            [('x', b) for b in range(8, NB)]
    assert Q == 4 and F == 256 and FO == 256 and F * SCALE ** 2 < 65504 ** 2 and NB == 16

    adj_v = adj.rearrange("(g t k e) (q c) -> t e q k g c", g=Q, k=K, e=2, q=Q)
    zt_v = out.rearrange("(g t k e) f -> t g k e f", g=Q, k=K, e=2)
    out_v = out.rearrange("(g t k e) f -> t g k e f", g=Q, k=K, e=2)
    xb_v = x.rearrange("(g b t k e) f -> b g k t (e f)", g=Q, b=NB, k=K, e=2)
    z_v = out.rearrange("(g b t k e) f -> b g k t (e f)", g=Q, b=NB, k=K, e=2)

    ctx = ExitStack()
    with ctx:
        def sb(name, shape, dt):
            return ctx.enter_context(nc.sbuf_tensor(name, shape, dt))

        def ps(name, shape, dt):
            return ctx.enter_context(nc.psum_tensor(name, shape, dt))

        def sem(name):
            return ctx.enter_context(nc.semaphore(name))

        gparts = sb("gparts", [P, NT, 2 * F], fp16)
        stage = sb("stage", [P, 2, 2, 2, C], i32)
        cast = sb("cast", [P, 2, C], fp16)
        adjT = sb("adjT", [P, 2, PAIRS, Q, K], u32)
        xlast = sb("xlast", [P, 4 * XB * F], fp32)
        work = sb("work", [P, 8 * F], fp32)
        regions = [adjT[:, 1].rearrange("p t g k -> p (t g k)").bitcast(fp32)] + \
                  [stage[:, 1, h].rearrange("p g c -> p (g c)").bitcast(fp32) for h in range(2)] + [xlast[:, :]]
        xb = [r.rearrange("p (n t f) -> p n t f", n=4, t=XB)[:, i] for r in regions for i in range(4)]
        wsb = xlast[:, 3 * XB * F:].rearrange("p (c s f) -> p c s f", c=FC, s=2)
        hf = work[:, :].rearrange("p (n t f) -> p n t f", n=4, t=2)
        zt = work[:, 0:2 * F].rearrange("p (n f) -> p n f", n=2)
        res = work[:, 2 * F:4 * F].rearrange("p (n f) -> p n f", n=2)
        low = work[:, 4 * F:5 * F]
        aggf = work[:, 5 * F:6 * F]
        zb = work[:, 6 * F:8 * F].rearrange("p (n f) -> p n f", n=2)
        hT = sb("hT", [P, 2, 2, FC, 2, P], fp16)
        wparts = sb("wparts", [P, 2, FC, 2 * FO], fp16)
        biasb = sb("biasb", [P, 2, FO], fp32)
        wmax = sb("wmax", [P, 1], fp32)
        wtop = sb("wtop", [P, 1], fp32)
        wpow = sb("wpow", [P, 1], fp32)
        wrec = sb("wrec", [P, 1], fp32)
        wscale = sb("wscale", [P, 1], fp32)
        unscale = sb("unscale", [P, 1], fp32)
        ident = sb("ident", [P, P], fp16)
        fold = sb("fold", [P, P], bf16)
        gmask = sb("gmask", [P, 3, Q], fp32)
        rowsum = sb("rowsum", [P, 2, Q], fp32)
        rest = sb("rest", [P, 2, Q], fp32)
        sumparts = sb("sumparts", [P, 2, 3, Q], bf16)
        zero = sb("zero", [P, Q], fp32)
        degq = sb("degq", [P, 3 * Q], fp32)
        deg = sb("deg", [P, 1], fp32)
        rdeg = sb("rdeg", [P, 2], fp32)
        stats = sb("stats", [P, 2, XB, 6], fp32)
        mv = sb("mv", [P, NB, XB, 2], fp32)
        var = sb("var", [P, NB, XB], fp32)
        mneg = sb("mneg", [P, NB, XB], fp32)
        std = sb("std", [P, NB, XB], fp32)
        r0 = sb("r0", [P, NB, XB], fp32)
        r1 = sb("r1", [P, NB, XB], fp32)
        rs = sb("rs", [P, NB, XB], fp32)
        nb = sb("nb", [P, NB, XB], fp32)

        p_agg0 = ps("p_agg0", [P, 2 * F], fp32)
        p_deg = ps("p_deg", [P, 512], fp32)
        p_t = [ps(f"p_t{i}", [P, 2, FC, 2, P], fp16) for i in range(2)]
        p_gz = [ps(f"p_gz{i}", [P, 2, 2 * FO], fp32) for i in range(2)]
        p_agg = [p_agg0, p_gz[0][:, 0]]

        adj16 = adjT[:, :, :, :, :].bitcast(fp16).rearrange("p s t g (k e) -> p s t (g k) e", e=2)
        cast32 = cast[:, :, :].bitcast(u32)

        x_in = [sem(f"x_in{b}") for b in range(NB)]
        w_in = sem("w_in")
        bias_in = sem("bias_in")
        staged = [[sem(f"staged{e}{h}") for h in range(2)] for e in range(2)]
        consts = sem("consts")
        cstep = sem("cstep")
        stats_v = sem("stats_v")
        std_ready = sem("std_ready")
        recip_ready = sem("recip_ready")
        wmax_ready = sem("wmax_ready")
        wtop_ready = sem("wtop_ready")
        wscale_ready = sem("wscale_ready")
        w_scaled = sem("w_scaled")
        w_high = sem("w_high")
        w_ready = sem("w_ready")
        norm_ready = sem("norm_ready")
        relu_done = sem("relu_done")
        high_done = sem("high_done")
        h_ready = sem("h_ready")
        hT_done = sem("hT_done")
        hT_ready = sem("hT_ready")
        gz_done = sem("gz_done")
        g_high = sem("g_high")
        z_done = sem("z_done")
        g_ready = sem("g_ready")
        z_sent = [sem(f"z_sent{r}") for r in range(4)]
        cast_done = sem("cast_done")
        group_done = sem("group_done")
        sums_split = sem("sums_split")
        deg_done = sem("deg_done")
        deg_read = sem("deg_read")
        deg_sum = sem("deg_sum")
        rdeg_ready = sem("rdeg_ready")
        agg_done = sem("agg_done")
        low_ready = sem("low_ready")
        agg_sum = sem("agg_sum")
        fin_done = sem("fin_done")
        z_in = sem("z_in")
        zb_ready = sem("zb_ready")
        sent = sem("sent")
        last_sent = sem("last_sent")
        split_step = sem("split_step")
        vstep = sem("vstep")

        def after(eng, s, v):
            if not isinstance(v, int) or v > 0:
                eng.wait_ge(s, v)

        def load_adj(eng, t, e, h, quadrants):
            for q in quadrants:
                eng.dma_start(stage[K * q:K * q + K, e, h, :, :],
                              adj_v[t, e, q, :, 2 * h:2 * h + 2, :]).then_inc(staged[e][h], 16)

        block = ctx.enter_context(nc.Block())

        @block.sync
        def _(sp):
            def load_x(b):
                if b == NB - 1:
                    sp.wait_ge(w_ready, 1)
                for g in (0, 2, 1, 3):
                    sp.dma_start(xb[b][K * g:K * g + K].rearrange("p (t e) f -> p t (e f)", e=2),
                                 xb_v[b, g]).then_inc(x_in[b], 16)

            def store_z(b):
                sp.wait_ge(z_done, 2 * b + 2)
                for g in (0, 2, 1, 3):
                    sp.dma_start(z_v[b, g], xb[b][K * g:K * g + K].rearrange("p (t e) f -> p t (e f)", e=2))\
                      .then_inc(z_sent[b // 4], 16)

            def load_tile(t, e, quadrants=(0, 1)):
                for h in range(2):
                    sp.wait_ge(cast_done, t * 8 + (4 * e + 2 * h + 2 - 8))
                    load_adj(sp, t, e, h, quadrants)

            def load_z(t):
                after(sp, zb_ready, t)
                for g in range(Q):
                    sp.dma_start(zt[K * g:K * g + K], zt_v[t, g]).then_inc(z_in, 16)

            load_x(0)
            for s in range(2):
                sp.dma_start(wsb[:, :, s, :], weight.rearrange("(s c p) f -> s p c f", s=2, p=P)[s]).then_inc(w_in, 16)
            for kind, i in ORDER:
                if kind == "x":
                    load_x(i)
                else:
                    load_adj(sp, 0, 0, i, (0, 2, 1, 3))
            for e in range(2):
                sp.dma_start(biasb[:, e], bias.rearrange("(a f) -> a f", a=1).broadcast_to([P, FO]))\
                  .then_inc(bias_in, 16)
            for b in range(NB):
                store_z(b)
                if b in (8, 12):
                    h = (b - 8) // 4
                    sp.wait_ge(z_sent[h + 1], 4 * 16 * Q)
                    load_adj(sp, 0, 1, h, (0, 2, 1, 3))
                if b == 5:
                    load_tile(1, 0, (0, 2, 1, 3))
            for r in range(4):
                sp.wait_ge(z_sent[r], 4 * 16 * Q)
            load_z(0)
            load_tile(1, 1, (0, 2, 1, 3))
            with sp.Fori(2, PAIRS) as t:
                load_tile(t, 0)
                load_z(t - 1)
                load_tile(t, 1)
            load_z(PAIRS - 1)
            for e in range(2):
                sp.wait_ge(fin_done, NT - 1 + e)
                for g in range(Q if e == 0 else Q // 2):
                    sp.dma_start(out_v[PAIRS - 1, g, :, e, :], res[K * g:K * g + K, e, :]).then_inc(last_sent, 16)
            sp.wait_ge(last_sent, 2 * 16 * Q)

        @block.gpsimd
        def _(pool):
            made = [0]

            def step(ins):
                made[0] += 1
                ins.then_inc(cstep, 1)
                pool.wait_ge(cstep, made[0])

            step(pool.memset(ident[:, :], 0.0))
            step(pool.memset(fold[:, :], 0.0))
            step(pool.memset(gmask[:, :, :], 0.0))
            step(pool.memset(zero[:, :], 0.0))
            for m, d in [(ident, 0)] + [(fold, d) for d in range(1 - Q, Q)]:
                step(pool.affine_select(out=m[:, :], in_=m[:, :], compare_op=ALU.not_equal, fill=1.0,
                                        base=-K * d, pattern=[[-1, P]], channel_multiplier=1))
            for g in range(Q):
                last = pool.memset(gmask[K * g:K * g + K, :, g], 1.0)
            last.then_inc(consts, 1)

            def norm_scale(b):
                pool.wait_ge(stats_v, b + 1)
                step(pool.tensor_scalar(mneg[:, b], mv[:, b, :, 0], -1.0, None, ALU.mult))
                pool.wait_ge(recip_ready, b + 1)
                step(pool.tensor_tensor(r1[:, b], r0[:, b], r0[:, b], ALU.mult))
                step(pool.tensor_tensor(r1[:, b], r1[:, b], var[:, b], ALU.mult))
                step(pool.tensor_scalar(r1[:, b], r1[:, b], -0.5 * SCALE, 1.5 * SCALE, ALU.mult, ALU.add))
                step(pool.tensor_tensor(rs[:, b], r1[:, b], r0[:, b], ALU.mult))
                pool.tensor_tensor(nb[:, b], mneg[:, b], rs[:, b], ALU.mult).then_inc(norm_ready, 1)

            def low_part(q):
                pool.wait_ge(high_done, q + 1)
                gp = gparts[:, 2 * q:2 * q + 2]
                pool.tensor_tensor(gp[:, :, F:2 * F], hf[:, q % 4], gp[:, :, 0:F], ALU.subtract).then_inc(h_ready, 1)

            def split_sums(t, e):
                pool.wait_ge(cast_done, t * 8 + (4 * e + 4))
                after(pool, deg_done, t * 2 + (e - 1))
                n = t * 8 + 4 * e
                rows, left, parts = rowsum[:, e], rest[:, e], sumparts[:, e]
                pool.tensor_tensor(parts[:, 0], rows, zero[:, :], ALU.add).then_inc(split_step, 1)
                pool.wait_ge(split_step, n + 1)
                pool.tensor_tensor(left, rows, parts[:, 0], ALU.subtract).then_inc(split_step, 1)
                pool.wait_ge(split_step, n + 2)
                pool.tensor_tensor(parts[:, 1], left, zero[:, :], ALU.add).then_inc(split_step, 1)
                pool.wait_ge(split_step, n + 3)
                pool.tensor_tensor(left, left, parts[:, 1], ALU.subtract).then_inc(split_step, 1)
                pool.wait_ge(split_step, n + 4)
                pool.tensor_tensor(parts[:, 2], left, zero[:, :], ALU.add).then_inc(sums_split, 1)

            for p in STEPS:
                if p == 1 - STATS:
                    pool.wait_ge(consts, 1)
                    pool.wait_ge(wmax_ready, 1)
                    pool.partition_all_reduce(wtop[:, :], wmax[:, :], P, bass.bass_isa.ReduceOp.max)\
                        .then_inc(wtop_ready, 1)
                if 0 <= p + LOW < PAIRS:
                    low_part(p + LOW)
                if (p + NORM) % 2 == 0 and 0 <= p + NORM < PAIRS:
                    norm_scale((p + NORM) // 2)
                if p == DEG_AT:
                    split_sums(0, 0)

            def add_bias(t):
                pool.wait_ge(z_in, t * (16 * Q) + 16 * Q)
                after(pool, fin_done, t * 2)
                pool.tensor_tensor(zb[:, :, :], zt[:, :, :], biasb[:, :, :], ALU.add).then_inc(zb_ready, 1)

            def send(t):
                pool.wait_ge(fin_done, t * 2 + 2)
                for g in range(Q):
                    pool.dma_start(out_v[t, g], res[K * g:K * g + K]).then_inc(sent, 16)

            split_sums(0, 1)
            pool.wait_ge(bias_in, 32)
            add_bias(0)
            split_sums(1, 0)
            split_sums(1, 1)
            send(0)
            with pool.Fori(2, PAIRS) as t:
                add_bias(t - 1)
                split_sums(t, 0)
                split_sums(t, 1)
                send(t - 1)
            add_bias(PAIRS - 1)
            pool.wait_ge(sent, 16 * Q * (PAIRS - 1))

        @block.scalar
        def _(act):
            def sqrt_var(b):
                act.wait_ge(stats_v, b + 1)
                nc.scalar.activation(std[:, b], var[:, b], ACT.Sqrt).then_inc(std_ready, 1)

            def relu(q):
                b = q // 2
                act.wait_ge(norm_ready, b + 1)
                after(act, h_ready, q - 3)
                for e in range(2):
                    i = 2 * (q % 2) + e
                    last = nc.scalar.activation(hf[:, q % 4, e], xb[b][:, i], ACT.Relu,
                                                bias=nb[:, b, i:i + 1], scale=rs[:, b, i:i + 1])
                last.then_inc(relu_done, 1)

            def copy_hT(q):
                act.wait_ge(hT_done, q + 1)
                after(act, gz_done, q - 1)
                nc.scalar.activation(hT[:, q % 2], p_t[q % 2][:, :, :, :, :], ACT.Copy).then_inc(hT_ready, 1)

            def high_g(q):
                act.wait_ge(z_done, q + 1)
                nc.scalar.activation(gparts[:, 2 * q:2 * q + 2, 0:F], p_gz[q % 2][:, :, 0:F], ACT.Copy,
                                     scale=1.0 / (SCALE * F)).then_inc(g_high, 1)

            def cast_group(t, e, g):
                if g % 2 == 0:
                    act.wait_ge(staged[e][g // 2], t * (16 * Q) + 16 * Q)
                after(act, group_done, t * 8 + (4 * e + g - 1))
                if g == 0:
                    after(act, sums_split, t * 2 + (e - 1))
                nc.scalar.activation(cast[:, g % 2], stage[:, e, g // 2, g % 2], ACT.Copy,
                                     accum_out=rowsum[:, e, g:g + 1]).then_inc(cast_done, 1)

            def scale_low(t, e):
                act.wait_ge(agg_done, t * 2 + (e + 1))
                act.wait_ge(rdeg_ready, t * 2 + (e + 1))
                after(act, agg_sum, t * 2 + e)
                nc.scalar.activation(low, p_agg[e][:, F:2 * F], ACT.Copy,
                                     scale=rdeg[:, e:e + 1]).then_inc(low_ready, 1)

            def load_half(t, e, h):
                act.wait_ge(cast_done, t * 8 + (4 * e + 2 * h + 2 - 8))
                load_adj(act, t, e, h, (2, 3))

            def tile(t, e, loading=True):
                cast_group(t, e, 0)
                cast_group(t, e, 1)
                scale_low(t - 1, e)
                if loading:
                    load_half(t + 1, e, 0)
                cast_group(t, e, 2)
                cast_group(t, e, 3)
                if loading:
                    load_half(t + 1, e, 1)

            for p in STEPS:
                if (p + NORM) % 2 == 0 and 0 <= p + NORM < PAIRS:
                    sqrt_var((p + NORM) // 2)
                if 0 <= p + EVAC < PAIRS:
                    high_g(p + EVAC)
                if 0 <= p + TRANS < PAIRS:
                    copy_hT(p + TRANS)
                if 0 <= p + RELU < PAIRS:
                    relu(p + RELU)
                if p == -RELU:
                    act.wait_ge(wscale_ready, 1)
                    nc.scalar.activation(wsb, wsb, ACT.Copy, scale=wscale[:, 0:1]).then_inc(w_scaled, 1)
                if p in CAST_AT:
                    cast_group(0, CAST_AT[p] // Q, CAST_AT[p] % Q)
            tile(1, 0)
            tile(1, 1)
            with act.Fori(2, PAIRS - 1) as t:
                tile(t, 0)
                tile(t, 1)
            tile(PAIRS - 1, 0, loading=False)
            tile(PAIRS - 1, 1, loading=False)
            for e in range(2):
                scale_low(PAIRS - 1, e)
            act.wait_ge(fin_done, NT)
            for g in range(Q // 2, Q):
                act.dma_start(out_v[PAIRS - 1, g, :, 1, :], res[K * g:K * g + K, 1, :]).then_inc(last_sent, 16)

        @block.vector
        def _(dve):
            steps = [0]

            def step(ins):
                steps[0] += 1
                ins.then_inc(vstep, 1)
                dve.wait_ge(vstep, steps[0])

            def norm_stats(q):
                b = q // 2
                if q % 2 == 0:
                    dve.wait_ge(x_in[b], 16 * Q)
                for i in range(2 * (q % 2), 2 * (q % 2) + 2):
                    last = nc.vector.bn_stats(stats[:, b % 2, i], xb[b][:, i])
                step(last)
                if q % 2 == 1:
                    for i in range(XB):
                        last = nc.vector.bn_aggr(mv[:, b, i], stats[:, b % 2, i])
                    step(last)
                    nc.vector.tensor_scalar(var[:, b], mv[:, b, :, 1], EPS, None, ALU.add).then_inc(stats_v, 1)

            def recip_std(b):
                dve.wait_ge(std_ready, b + 1)
                nc.vector.reciprocal(r0[:, b], std[:, b]).then_inc(recip_ready, 1)

            def high_part(q):
                dve.wait_ge(relu_done, q + 1)
                nc.vector.tensor_copy(gparts[:, 2 * q:2 * q + 2, 0:F], hf[:, q % 4]).then_inc(high_done, 1)

            def make_z(q):
                dve.wait_ge(gz_done, q + 1)
                z = xb[q // 2][:, 2 * (q % 2):2 * (q % 2) + 2]
                nc.vector.scalar_tensor_tensor(out=z, in0=p_gz[q % 2][:, :, FO:2 * FO], scalar=unscale[:, 0:1],
                                               in1=z, op0=ALU.mult, op1=ALU.add).then_inc(z_done, 1)

            def low_g(q):
                dve.wait_ge(g_high, q + 1)
                gp = gparts[:, 2 * q:2 * q + 2]
                nc.vector.scalar_tensor_tensor(out=gp[:, :, F:2 * F], in0=p_gz[q % 2][:, :, 0:F],
                                               scalar=1.0 / (SCALE * F), in1=gp[:, :, 0:F],
                                               op0=ALU.mult, op1=ALU.subtract).then_inc(g_ready, 1)

            def transpose_group(t, e, g):
                dve.wait_ge(cast_done, t * 8 + (4 * e + g + 1))
                if g == 0:
                    after(dve, agg_done, t * 2 + (e - 1))
                nc.vector.transpose(adjT[:, e, :, g, :], cast32[:, g % 2].rearrange("p (t k) -> p t k", k=K))\
                  .then_inc(group_done, 1)

            def degree(t, e):
                dve.wait_ge(deg_done, t * 2 + (e + 1))
                nc.vector.tensor_tensor(degq[:, :], p_deg[:, 0:3 * Q], gmask[:, :, :].rearrange("p a g -> p (a g)"),
                                        ALU.mult).then_inc(deg_read, 1)
                dve.wait_ge(deg_read, t * 2 + (e + 1))
                nc.vector.reduce_sum(deg[:, :], degq[:, :], axis=mybir.AxisListType.X).then_inc(deg_sum, 1)
                dve.wait_ge(deg_sum, t * 2 + (e + 1))
                nc.vector.reciprocal(rdeg[:, e:e + 1], deg[:, :]).then_inc(rdeg_ready, 1)

            def finish(t, e):
                n = t * 2 + (e + 1)
                dve.wait_ge(low_ready, n)
                nc.vector.scalar_tensor_tensor(out=aggf, in0=p_agg[e][:, 0:F], scalar=rdeg[:, e:e + 1],
                                               in1=low, op0=ALU.mult, op1=ALU.add).then_inc(agg_sum, 1)
                dve.wait_ge(agg_sum, n)
                if e == 0:
                    dve.wait_ge(zb_ready, t + 1)
                    after(dve, sent, t * (16 * Q))
                nc.vector.tensor_tensor(res[:, e], aggf, zb[:, e], ALU.add).then_inc(fin_done, 1)

            def largest_weight():
                dve.wait_ge(w_in, 32)
                nc.vector.tensor_reduce(wmax[:, :], wsb.rearrange("p c s f -> p (c s) f"), mybir.AxisListType.XY,
                                        ALU.max, apply_absolute_value=True).then_inc(wmax_ready, 1)

            def scale_factors():
                dve.wait_ge(wtop_ready, 1)
                step(nc.vector.tensor_scalar(wtop[:, :], wtop[:, :], 2.0 ** -100, None, ALU.max))
                step(nc.vector.tensor_scalar(wpow[:, :].bitcast(i32), wtop[:, :].bitcast(i32), 0x7F800000, None,
                                             ALU.bitwise_and))
                step(nc.vector.reciprocal(wrec[:, :], wpow[:, :]))
                step(nc.vector.tensor_scalar(wscale[:, :], wrec[:, :], 2.0 ** 14, None, ALU.mult))
                nc.vector.tensor_scalar(unscale[:, :], wpow[:, :], 2.0 ** -14 / SCALE, None, ALU.mult)\
                  .then_inc(wscale_ready, 1)
                dve.wait_ge(consts, 1)
                step(nc.vector.tensor_scalar(gmask[:, :, :], gmask[:, :, :], wscale[:, 0:1], 1.0 / F,
                                             ALU.mult, ALU.mult))

            def split_weight(part):
                wp = wparts.rearrange("p a c (s f) -> p a c s f", s=2)
                if part == 0:
                    dve.wait_ge(w_scaled, 1)
                    nc.vector.tensor_copy(wp[:, 0], wsb).then_inc(w_high, 1)
                else:
                    dve.wait_ge(w_high, 1)
                    nc.vector.tensor_tensor(wp[:, 1], wsb, wp[:, 0], ALU.subtract).then_inc(w_ready, 1)

            def tile(t, e):
                transpose_group(t, e, 0)
                finish(t - 1, e)
                transpose_group(t, e, 1)
                degree(t - 1 + e, 1 - e)
                transpose_group(t, e, 2)
                transpose_group(t, e, 3)

            for p in STEPS:
                if p == 2 - STATS:
                    largest_weight()
                if p == 3 - STATS:
                    scale_factors()
                if 0 <= p + EVAC < PAIRS:
                    make_z(p + EVAC)
                if 0 <= p + HIGH < PAIRS:
                    high_part(p + HIGH)
                    if p + HIGH < 2:
                        split_weight(p + HIGH)
                if (p + NORM) % 2 == 0 and 0 <= p + NORM < PAIRS:
                    recip_std((p + NORM) // 2)
                if 0 <= p + STATS < PAIRS:
                    norm_stats(p + STATS)
                if 0 <= p + EVAC < PAIRS:
                    low_g(p + EVAC)
                if p - 1 in CAST_AT:
                    if CAST_AT[p - 1] == Q:
                        dve.wait_ge(z_sent[0], 4 * 16 * Q)
                    transpose_group(0, CAST_AT[p - 1] // Q, CAST_AT[p - 1] % Q)
                if p == DEG_AT + 2:
                    degree(0, 0)

            def late_tile(t, e):
                for g in range(Q):
                    transpose_group(t, e, g)
                finish(t - 1, e)
                degree(t - 1 + e, 1 - e)

            late_tile(1, 0)
            tile(1, 1)
            late_tile(2, 0)
            tile(2, 1)
            with dve.Fori(3, PAIRS) as t:
                tile(t, 0)
                tile(t, 1)
            finish(PAIRS - 1, 0)
            degree(PAIRS - 1, 1)
            finish(PAIRS - 1, 1)

        @block.tensor
        def _(pe):
            def products(e, tiles):
                for j in tiles:
                    last = nc.tensor.matmul(p_agg[e][:, :], adj16[:, e, j // 2, :, j % 2], gparts[:, j, :],
                                            start=(j == 0), stop=(j == NT - 1))
                if tiles[-1] == NT - 1:
                    last.then_inc(agg_done, 1)

            def degree(t, e):
                pe.wait_ge(sums_split, t * 2 + (e + 1))
                after(pe, deg_read, t * 2 + e)
                nc.tensor.matmul(p_deg[:, 0:3 * Q], fold[:, :], sumparts[:, e].rearrange("p a g -> p (a g)"),
                                 start=True, stop=True).then_inc(deg_done, 1)

            def transpose_h(q):
                pe.wait_ge(h_ready, q + 1)
                after(pe, hT_ready, q - 1)
                for e in range(2):
                    for c in range(FC):
                        for part in range(2):
                            last = nc.tensor.transpose(
                                p_t[q % 2][:, e, c, part, :],
                                gparts[:, 2 * q + e, part * F + c * P:part * F + (c + 1) * P], ident[:, :])
                last.then_inc(hT_done, 1)

            def weigh(q):
                pe.wait_ge(hT_ready, q + 1)
                after(pe, g_ready, q - 1)
                terms = [(c, a, b) for c in range(FC) for a, b in ((0, 0), (1, 0), (0, 1))]
                for e in range(2):
                    for n, (c, a, b) in enumerate(terms):
                        last = nc.tensor.matmul(p_gz[q % 2][:, e], hT[:, q % 2, e, c, a, :], wparts[:, b, c, :],
                                                start=(n == 0), stop=(n == len(terms) - 1))
                last.then_inc(gz_done, 1)

            def tile(t, e, degrees):
                pe.wait_ge(group_done, t * 8 + (4 * e + 4))
                after(pe, agg_sum, t * 2 + (e - 1))
                at = 0
                for j, t_d, e_d in degrees:
                    products(e, range(at, j))
                    degree(t_d, e_d)
                    at = j
                products(e, range(at, NT))

            def steady(t, e):
                tile(t, e, [(56, t + e, 1 - e)])

            pe.wait_ge(consts, 1)
            for p in range(-TRANS, PAIRS - AGG):
                if 0 <= p + TRANS < PAIRS:
                    transpose_h(p + TRANS)
                if p == 0:
                    pe.wait_ge(w_ready, 1)
                if 0 <= p < PAIRS:
                    weigh(p)
                if p == DEG_AT + 1:
                    degree(0, 0)
                q = p + AGG
                if q == 0:
                    pe.wait_ge(group_done, Q)
                if 0 <= q < PAIRS:
                    pe.wait_ge(g_ready, q + 1)
                    products(0, [2 * q, 2 * q + 1])
            tile(0, 1, [(8, 0, 1), (56, 1, 0)])
            steady(1, 0)
            steady(1, 1)
            with pe.Fori(2, PAIRS - 1) as t:
                steady(t, 0)
                steady(t, 1)
            steady(PAIRS - 1, 0)
            tile(PAIRS - 1, 1, [])


_INS = ['x', 'adj', 'L0_gnn_weight', 'L0_gnn_bias']
_OUTS = [((8192, 256), 'float32')]


def kernel(**inputs):
    import numpy as _np
    import concourse.bacc as _bacc
    from concourse import mybir as _mybir
    from concourse.bass_utils import run_bass_kernel_spmd as _run

    nc = _bacc.Bacc("TRN2", target_bir_lowering=False, num_devices=1)
    arrays, args = {}, []
    for name in _INS:
        a = _np.ascontiguousarray(inputs[name])
        arrays[f"in_{name}_dram"] = a
        args.append(nc.dram_tensor(f"in_{name}_dram", a.shape, _mybir.dt.from_np(a.dtype), kind="ExternalInput").ap())
    for i, (shape, dtype) in enumerate(_OUTS):
        dt = _mybir.dt.from_np(_np.dtype(dtype))
        args.append(nc.dram_tensor(f"out_{i}_dram", shape, dt, kind="ExternalOutput").ap())
    graph_layer_kernel(nc, *args)
    r = _run(nc, [arrays], core_ids=[0])
    return r.results[0]["out_0_dram"]
```
